# Optimizing a Trainium2 kernel written in Bass

```python
import numpy as np
import jax
import jax.numpy as jnp

def _softmax(x, axis=-1):
    return jax.nn.softmax(x, axis=axis)

def _gelu(x):
    return jax.nn.gelu(x, approximate=True)

def _silu(x):
    return jax.nn.silu(x)

def _sigmoid(x):
    return jax.nn.sigmoid(x)

def _layernorm(x, axis=-1, eps=1e-05):
    m = jnp.mean(x, axis=axis, keepdims=True)
    v = jnp.var(x, axis=axis, keepdims=True)
    return (x - m) / jnp.sqrt(v + eps)

def _scatter_add(tgt, idx, src, axis=0):
    return tgt.at[idx].add(src)

def _segment_sum(src, seg, n):
    return jax.ops.segment_sum(src, seg, n)
kernel_name = 'mk_gnn_preln_d2_gnn_r8_2dc41a'

def setup_inputs(seed: int=0):
    np.random.seed(seed)
    _w = jnp.asarray

    def _rec_inputs():
        import jax
        import jax.numpy as jnp
        _gk = jax.random.key(seed)
        x = -0.000202 + 1 * jax.random.normal(jax.random.fold_in(_gk, 1), (12500, 128), jnp.float32)
        src = jax.random.randint(jax.random.fold_in(_gk, 2), (400000,), 0, 12500, jnp.int32)
        dst = jax.random.randint(jax.random.fold_in(_gk, 3), (400000,), 0, 12500, jnp.int32)
        _o = jnp.argsort(dst, stable=True)
        src = src[_o]
        dst = dst[_o]
        edge_attr_42 = 0.000171677 + 1.0001 * jax.random.normal(jax.random.fold_in(_gk, 11), (400000, 42), jnp.float32)
        edge_weight = jax.random.uniform(jax.random.fold_in(_gk, 13), (400000,), jnp.float32, 0.0, 0.999998)
        node_vec = jax.random.uniform(jax.random.fold_in(_gk, 14), (12500,), jnp.float32, 0.0, 0.999994)
        return (x, src, dst, edge_attr_42, edge_weight, node_vec)
    x, src, dst, edge_attr_42, edge_weight, node_vec = _rec_inputs()

    def _L0_gnn_setup():
        import jax, jax.numpy as jnp
        import numpy as np
        NODE_EMB_DIM = 16
        NUM_REL = 10

        def _rgcn_layer(x, src, dst, edge_type, w_rel, root, bias):
            N = x.shape[0]
            seg = dst * NUM_REL + edge_type
            xs = x[src]
            sums = jax.ops.segment_sum(xs, seg, num_segments=N * NUM_REL)
            cnt = jax.ops.segment_sum(jnp.ones(seg.shape, x.dtype), seg, num_segments=N * NUM_REL)
            mean = (sums / jnp.maximum(cnt, 1.0)[:, None]).reshape(N, NUM_REL, -1)
            return jnp.einsum('nrd,rdo->no', mean, w_rel) + x @ root + bias
        key = jax.random.key(seed)
        ks = jax.random.split(key, 10)
        N, E, C = (6250, 100000, 128)
        s = 1.0 / np.sqrt(C).astype(np.float32)
        x = jax.random.normal(ks[0], (N, C), jnp.float32)
        last_update = jax.random.uniform(ks[1], (N,), jnp.float32)
        t = jax.random.uniform(ks[2], (E,), jnp.float32)
        msg = jax.random.normal(ks[3], (E, 2 * NODE_EMB_DIM + NUM_REL), jnp.float32)
        w_rel1 = jax.random.normal(ks[4], (NUM_REL, C, C), jnp.float32) * s
        root1 = jax.random.normal(ks[5], (C, C), jnp.float32) * s
        b1 = jnp.zeros((C,), jnp.float32)
        w_rel2 = jax.random.normal(ks[6], (NUM_REL, C, C), jnp.float32) * s
        root2 = jax.random.normal(ks[7], (C, C), jnp.float32) * s
        b2 = jnp.zeros((C,), jnp.float32)
        edge_index = jax.random.randint(ks[8], (2, E), 0, N, dtype=jnp.int32)
        return dict(x=x, last_update=last_update, t=t, msg=msg, w_rel1=w_rel1, root1=root1, b1=b1, w_rel2=w_rel2, root2=root2, b2=b2, edge_index=edge_index)
    _L0_gnn_all = _L0_gnn_setup()
    _L0_gnn_in = {k: v for k, v in _L0_gnn_all.items() if k in ('w_rel1', 'root1', 'b1', 'w_rel2', 'root2', 'b2')}
    del _L0_gnn_all

    def _L1_gnn_setup():
        import jax, jax.numpy as jnp
        import numpy as np
        N, E = (12500, 200000)
        D_IN, H, C = (128, 4, 32)
        NEG_SLOPE = 0.2
        key = jax.random.key(seed)
        ks = jax.random.split(key, 6)
        x = jax.random.normal(ks[0], (N, D_IN), dtype=jnp.float32)
        edge_index = jax.random.randint(ks[1], (2, E), 0, N, dtype=jnp.int64)
        s = 1.0 / np.sqrt(D_IN)
        W_l = jax.random.normal(ks[2], (D_IN, H * C), dtype=jnp.float32) * s
        W_r = jax.random.normal(ks[3], (D_IN, H * C), dtype=jnp.float32) * s
        att = jax.random.normal(ks[4], (H, C), dtype=jnp.float32) * (1.0 / np.sqrt(C))
        bias = jax.random.normal(ks[5], (H * C,), dtype=jnp.float32) * 0.01
        return {'x': x, 'edge_index': edge_index, 'W_l': W_l, 'W_r': W_r, 'att': att, 'bias': bias}
    _L1_gnn_all = _L1_gnn_setup()
    _L1_gnn_in = {k: v for k, v in _L1_gnn_all.items() if k in ('W_l', 'W_r', 'att', 'bias')}
    del _L1_gnn_all
    return {'x': x, 'src': src, 'dst': dst, 'edge_attr_42': edge_attr_42, 'edge_weight': edge_weight, 'node_vec': node_vec, 'L0_gnn_w_rel1': _L0_gnn_in['w_rel1'], 'L0_gnn_root1': _L0_gnn_in['root1'], 'L0_gnn_b1': _L0_gnn_in['b1'], 'L0_gnn_w_rel2': _L0_gnn_in['w_rel2'], 'L0_gnn_root2': _L0_gnn_in['root2'], 'L0_gnn_b2': _L0_gnn_in['b2'], 'L1_gnn_W_l': _L1_gnn_in['W_l'], 'L1_gnn_W_r': _L1_gnn_in['W_r'], 'L1_gnn_att': _L1_gnn_in['att'], 'L1_gnn_bias': _L1_gnn_in['bias']}

def reference(x, src, dst, edge_attr_42, edge_weight, node_vec, L0_gnn_w_rel1, L0_gnn_root1, L0_gnn_b1, L0_gnn_w_rel2, L0_gnn_root2, L0_gnn_b2, L1_gnn_W_l, L1_gnn_W_r, L1_gnn_att, L1_gnn_bias):
    import jax
    import jax.numpy as jnp

    def _L0_gnn_ref(x, last_update, t, msg, w_rel1, root1, b1, w_rel2, root2, b2, edge_index):
        import jax, jax.numpy as jnp
        import numpy as np
        NODE_EMB_DIM = 16
        NUM_REL = 10

        def _rgcn_layer(x, src, dst, edge_type, w_rel, root, bias):
            N = x.shape[0]
            seg = dst * NUM_REL + edge_type
            xs = x[src]
            sums = jax.ops.segment_sum(xs, seg, num_segments=N * NUM_REL)
            cnt = jax.ops.segment_sum(jnp.ones(seg.shape, x.dtype), seg, num_segments=N * NUM_REL)
            mean = (sums / jnp.maximum(cnt, 1.0)[:, None]).reshape(N, NUM_REL, -1)
            return jnp.einsum('nrd,rdo->no', mean, w_rel) + x @ root + bias
        src, dst = (edge_index[0], edge_index[1])
        edge_type = jnp.argmax(msg[:, NODE_EMB_DIM:-NODE_EMB_DIM], axis=1).astype(jnp.int32)
        h = jax.nn.relu(_rgcn_layer(x, src, dst, edge_type, w_rel1, root1, b1))
        return _rgcn_layer(h, src, dst, edge_type, w_rel2, root2, b2)

    def _L1_gnn_ref(x, edge_index, W_l, W_r, att, bias):
        import jax, jax.numpy as jnp
        import numpy as np
        N, E = (12500, 200000)
        D_IN, H, C = (128, 4, 32)
        NEG_SLOPE = 0.2
        src, dst = (edge_index[0], edge_index[1])
        n = x.shape[0]
        xl = (x @ W_l).reshape(n, H, C)
        xr = (x @ W_r).reshape(n, H, C)
        xj = xl[src]
        xi = xr[dst]
        e = jax.nn.leaky_relu(xi + xj, NEG_SLOPE)
        score = jnp.einsum('ehc,hc->eh', e, att)
        m = jax.ops.segment_max(score, dst, num_segments=n)
        ex = jnp.exp(score - m[dst])
        denom = jax.ops.segment_sum(ex, dst, num_segments=n)
        alpha = ex / (denom[dst] + 1e-16)
        out = jax.ops.segment_sum(alpha[..., None] * xj, dst, num_segments=n)
        return out.reshape(n, H * C) + bias
    edge_index = jnp.stack([src, dst])
    h = jnp.maximum(_layernorm(x, axis=-1), 0.0)
    x = x + _L0_gnn_ref(h, node_vec, edge_weight, edge_attr_42, L0_gnn_w_rel1, L0_gnn_root1, L0_gnn_b1, L0_gnn_w_rel2, L0_gnn_root2, L0_gnn_b2, edge_index)
    h = jnp.maximum(_layernorm(x, axis=-1), 0.0)
    x = x + _L1_gnn_ref(h, edge_index, L1_gnn_W_l, L1_gnn_W_r, L1_gnn_att, L1_gnn_bias)
    return x

_drawn_inputs = setup_inputs


def setup_inputs(seed=0):
    import zlib

    import numpy as np

    out = dict(_drawn_inputs(seed))
    spreads = {'L0_gnn_b1': (0.0, 0.1), 'L0_gnn_b2': (0.0, 0.346)}
    factors = {'L1_gnn_W_r': 8.0, 'L1_gnn_att': 8.0, 'L1_gnn_bias': 8.0}
    for name, (base, spread) in spreads.items():
        noise = np.random.default_rng([zlib.crc32(name.encode()), seed]).standard_normal(out[name].shape)
        drawn = base * np.exp(spread * noise) if base else spread * noise
        out[name] = jnp.asarray(drawn.astype(out[name].dtype))
    for name, factor in factors.items():
        out[name] = (out[name] * factor).astype(out[name].dtype)
    return out
```

```python
from contextlib import ExitStack

import concourse.bass as bass
from concourse import mybir

F32 = mybir.dt.float32
BF16 = mybir.dt.bfloat16
I32 = mybir.dt.int32
ALU = mybir.AluOpType
ACT = mybir.ActivationFunctionType
AX = mybir.AxisListType.X
ds = bass.ds

P = 128
N = 12500
D = 128
E = 400000
NREL, ATTR, EMB = 10, 42, 16
H, C = 4, 32
SLOPE, EPS = 0.2, 1e-5

NT = -(-N // P)
LAST = N - (NT - 1) * P
TILES = E // P
G = 5
GROUPS = TILES // G
GE = G * P
STEPS = GROUPS + NT - 1
SLOTS = 5
ROUNDS = GROUPS // SLOTS
CH = 125
CT = TILES // CH
CE = CT * P
SCOLS = -(-STEPS // P)
BIG = 3.0e38
GD = G * D
W = D + H
ALL = NREL * D + D
assert E == TILES * P and TILES == GROUPS * G and GROUPS == ROUNDS * SLOTS and TILES == CH * CT
assert STEPS % 2 == 0 and NT % 2 == 0


def build(nc, x, src, dst, attr, w_rel1, root1, b1, w_rel2, root2, b2, w_l, w_r, att, bias, out,
          ytab, xltab, x1_dram, xj_dram, step_dram, base_dram, stop=99):
    outer = ExitStack()

    def sem(name):
        return outer.enter_context(nc.semaphore(name))

    def sbuf(stack, name, shape, dt=F32):
        return stack.enter_context(nc.sbuf_tensor(name, shape, dt))

    def psum(stack, name, shape, dt=F32):
        return stack.enter_context(nc.psum_tensor(name, shape, dt))

    passed = {}

    def gate(eng, name, *waits):
        if name not in passed:
            passed[name] = sem(f"gate_{name}")
        for s, v in waits:
            eng.wait_ge(s, v)
        eng.sem_inc(passed[name])

    class Chain:

        def __init__(self, eng, name):
            self.eng, self.sem, self.n = eng, sem(name), 0

        def __call__(self, ins):
            self.n += 1
            ins.then_inc(self.sem, 1)
            self.eng.wait_ge(self.sem, self.n)

    with outer:
        A = sbuf(outer, "A", [P, NT * W])
        dst_f = sbuf(outer, "dst_f", [P, TILES])
        src_i = sbuf(outer, "src_i", [P, CE], I32)
        steps = sbuf(outer, "steps", [1, 4 * SCOLS * P], I32)
        done = sbuf(outer, "done", [1, GROUPS], I32)
        base = sbuf(outer, "base", [P, SCOLS * P])
        ident = sbuf(outer, "ident", [P, P])
        cols = sbuf(outer, "cols", [P, P])
        rowid = sbuf(outer, "rowid", [P, 1])

        relational = outer.enter_context(ExitStack())
        rel_i = sbuf(relational, "rel_i", [P, TILES + SLOTS * G], I32)
        wgt = sbuf(relational, "wgt", [P, TILES])

        with ExitStack() as st:
            ea = [sbuf(st, f"ea{k}", [CH, P * ATTR]) for k in range(2)]
            top = sbuf(st, "top", [CH, P])
            vote = sbuf(st, "vote", [CH, P * NREL])
            falling = sbuf(st, "falling", [CH, NREL])
            raw = src_i[0:CH, :]
            relc = sbuf(st, "relc", [CH, CE], BF16)
            same = sbuf(st, "same", [CH, CE + 1], BF16)
            firstm = sbuf(st, "firstm", [CH, CE], BF16)
            lastm = sbuf(st, "lastm", [CH, CE], BF16)
            dstc, fwd, bwd, tot = (A[0:CH, k * CE:(k + 1) * CE] for k in range(4))
            edge_i = sbuf(st, "edge_i", [CH, 2], I32)
            edge_f = sbuf(st, "edge_f", [CH, 2])
            ends = sbuf(st, "ends", [CH, 4 * NREL])
            endt = sbuf(st, "endt", [NREL, 4, CH])
            carry = sbuf(st, "carry", [NREL, 2, CH + 1])
            carc = sbuf(st, "carc", [CH, 2, NREL])
            last_i = sbuf(st, "last_i", [1, GROUPS], I32)
            last_t = sbuf(st, "last_t", [1, GROUPS], I32)
            gnum = sbuf(st, "gnum", [1, GROUPS])
            fin = sbuf(st, "fin", [1, GROUPS])
            ones = sbuf(st, "ones", [1, P])
            snum = sbuf(st, "snum", [P, SCOLS])
            junk = sbuf(st, "junk", [P, GROUPS])
            gs = sbuf(st, "gs", [P, SCOLS])
            ns = sbuf(st, "ns", [P, SCOLS])
            ring = sbuf(st, "ring", [P, 2, SCOLS])
            ring_i = sbuf(st, "ring_i", [P, SCOLS], I32)
            tab = sbuf(st, "tab", [P, SCOLS, 4], I32)
            tabf = sbuf(st, "tabf", [P, SCOLS])
            ps = [psum(st, f"ps{k}", [P, 8, P]) for k in range(2)]
            psf = psum(st, "psf", [P, 1024])

            s_ea = [sem(f"ea_in{k}") for k in range(2)]
            s_dst, s_src, s_nb = sem("dst_in"), sem("src_in"), sem("neighbours_in")
            s_last, s_rel, s_iota = sem("last_in"), sem("ea_used"), sem("iotas")
            s_const, s_raw = sem("prep_const"), sem("raw_free")
            s_tp, s_ev, s_pe = sem("turned"), sem("to_turn"), sem("psum_free")
            s_tab, s_step = sem("tables_made"), sem("tables_moved")

            with nc.Block() as block:

                @block.sync
                def _(sp):
                    av = attr.rearrange("(p t e) a -> p t (e a)", t=CT, e=P)
                    sp.dma_start(raw[:, :], dst.rearrange("(p e) -> p e", p=CH)).then_inc(s_dst, 16)
                    with nc.allow_non_contiguous_dma(reason="one destination of each group and chunk"):
                        sp.dma_start(last_i[:, :], dst.rearrange("(a g e) -> a g e", a=1, e=GE)[:, :, GE - 1]).then_inc(s_last, 16)
                        sp.wait_ge(s_const, 1)
                        sp.dma_start(edge_i[1:CH, 0:1], dst.rearrange("(p e) -> p e", p=CH)[0:CH - 1, CE - 1:CE]).then_inc(s_nb, 16)
                        sp.dma_start(edge_i[0:CH - 1, 1:2], dst.rearrange("(p e) -> p e", p=CH)[1:CH, 0:1]).then_inc(s_nb, 16)
                    for t in range(CT):
                        if t >= 2:
                            sp.wait_ge(s_rel, t - 1)
                        sp.dma_start(ea[t % 2][:, :], av[:, t, :]).then_inc(s_ea[t % 2], 16)
                        if t == 2:
                            sp.wait_ge(s_raw, 1)
                            sp.dma_start(raw[:, :], src.rearrange("(p e) -> p e", p=CH)).then_inc(s_src, 16)
                    sp.wait_ge(s_tab, 1)
                    sp.dma_start(step_dram.rearrange("(c p) k -> p c k", p=P), tab[:, :, :]).then_inc(s_step, 16)
                    with nc.allow_non_contiguous_dma(reason="a column per 128 steps"):
                        sp.dma_start(base_dram.rearrange("(c p) -> p c", p=P), tabf[:, :]).then_inc(s_step, 16)
                    sp.wait_ge(s_step, 32)
                    sp.dma_start(steps[:, :], step_dram.rearrange("(a s) k -> a (s k)", a=1)).then_inc(s_step, 16)
                    sp.dma_start(base[:, :], base_dram.rearrange("(a s) -> a s", a=1).to_broadcast([P, SCOLS * P])).then_inc(s_step, 16)
                    sp.wait_ge(s_step, 64)

                @block.gpsimd
                def _(pool):
                    nc.gpsimd.iota(cols[:, :], [[1, P]], base=0, channel_multiplier=0, allow_small_or_imprecise_dtypes=True).then_inc(s_iota, 1)
                    nc.gpsimd.iota(rowid[:, :], [[0, 1]], base=0, channel_multiplier=1, allow_small_or_imprecise_dtypes=True).then_inc(s_iota, 1)
                    nc.gpsimd.iota(falling[:, :], [[-1, NREL]], base=NREL, channel_multiplier=0, allow_small_or_imprecise_dtypes=True).then_inc(s_iota, 1)
                    nc.gpsimd.iota(gnum[:, :], [[1, GROUPS]], base=0, channel_multiplier=0, allow_small_or_imprecise_dtypes=True).then_inc(s_iota, 1)
                    nc.gpsimd.iota(snum[:, :], [[P, SCOLS]], base=0, channel_multiplier=1, allow_small_or_imprecise_dtypes=True).then_inc(s_iota, 1)
                    nc.gpsimd.memset(rel_i[:, TILES:], 0).then_inc(s_iota, 1)

                @block.vector
                def _(dve):
                    link = Chain(dve, "prep_chain")
                    v = nc.vector
                    link(v.memset(ones[:, :], 1.0))
                    v.memset(edge_i[:, :], -1).then_inc(s_const, 1)
                    dve.wait_ge(s_iota, 6)
                    link(v.tensor_scalar(ident[:, :], cols[:, :], rowid[:, 0:1], None, ALU.is_equal))

                    dve.wait_ge(s_last, 16)
                    link(v.tensor_scalar(last_t[:, :], last_i[:, :], 7, None, ALU.arith_shift_right))
                    link(v.tensor_tensor(fin[:, :], last_t[:, :], gnum[:, :], ALU.add))
                    link(v.tensor_scalar(done[:, :], fin[:, :], 1.0, None, ALU.add))
                    v.engine_nop().then_inc(s_ev, 1)
                    dve.wait_ge(s_tp, 1)
                    for c in range(SCOLS):
                        link(v.tensor_scalar(junk[:, :], psf[:, 0:GROUPS], snum[:, c:c + 1], 0.0, ALU.is_lt, ALU.add,
                                             accum_out=gs[:, c:c + 1]))
                    link(v.tensor_scalar(gs[:, :], gs[:, :], float(GROUPS - 1), None, ALU.min))
                    link(v.tensor_tensor(ns[:, :], snum[:, :], gs[:, :], ALU.subtract))
                    link(v.tensor_scalar(tab[:, :, 0], gs[:, :], 1.0, None, ALU.add))
                    link(v.tensor_scalar(tab[:, :, 2], gs[:, :], float(G), None, ALU.mult))
                    link(v.tensor_scalar(ns[:, :], ns[:, :], float(NT - 1), None, ALU.min))
                    link(v.tensor_copy(tab[:, :, 3], ns[:, :]))
                    link(v.tensor_scalar(tabf[:, :], ns[:, :], float(P), None, ALU.mult))
                    link(v.tensor_copy(ring[:, 0, :], gs[:, :]))
                    for step in ring_steps():
                        link(v.tensor_scalar(ring[:, 1, :], ring[:, 0, :], float(step), float(step), ALU.is_ge, ALU.mult))
                        link(v.tensor_tensor(ring[:, 0, :], ring[:, 0, :], ring[:, 1, :], ALU.subtract))
                    link(v.tensor_copy(tab[:, :, 1], ring[:, 0, :]))
                    v.engine_nop().then_inc(s_tab, 1)

                    dve.wait_ge(s_dst, 16)
                    link(v.tensor_copy(dstc, raw[:, :]))
                    v.engine_nop().then_inc(s_raw, 1)
                    dve.wait_ge(s_nb, 32)
                    link(v.tensor_copy(edge_f[:, :], edge_i[:, :]))
                    link(v.tensor_tensor(same[:, 1:CE], dstc[:, 1:CE], dstc[:, 0:CE - 1], ALU.is_equal))
                    link(v.tensor_scalar(same[:, 0:1], dstc[:, 0:1], edge_f[:, 0:1], None, ALU.is_equal))
                    link(v.tensor_scalar(same[:, CE:CE + 1], dstc[:, CE - 1:CE], edge_f[:, 1:2], None, ALU.is_equal))
                    link(v.tensor_scalar(firstm[:, :], dstc, dstc[:, 0:1], None, ALU.is_equal))
                    link(v.tensor_scalar(lastm[:, :], dstc, dstc[:, CE - 1:CE], None, ALU.is_equal))
                    link(v.tensor_scalar(ends[:, 2 * NREL:3 * NREL], dstc[:, CE - NREL:CE], 0.0, dstc[:, CE - 1:CE], ALU.mult, ALU.add))
                    link(v.tensor_scalar(ends[:, 2 * NREL:3 * NREL], ends[:, 2 * NREL:3 * NREL], edge_f[:, 0:1], None, ALU.is_equal))
                    link(v.tensor_scalar(ends[:, 3 * NREL:4 * NREL], dstc[:, 0:NREL], 0.0, dstc[:, 0:1], ALU.mult, ALU.add))
                    link(v.tensor_scalar(ends[:, 3 * NREL:4 * NREL], ends[:, 3 * NREL:4 * NREL], edge_f[:, 1:2], None, ALU.is_equal))

                    for t in range(CT):
                        dve.wait_ge(s_ea[t % 2], 16 * (t // 2 + 1))
                        a = ea[t % 2][:, :].rearrange("p (e a) -> p e a", a=ATTR)[:, :, EMB:EMB + NREL]
                        vv = vote[:, :].rearrange("p (e r) -> p e r", r=NREL)
                        link(v.tensor_reduce(top[:, :], a, AX, ALU.max))
                        link(v.tensor_tensor(vv, a, top[:, :].rearrange("p (e a) -> p e a", a=1).to_broadcast([CH, P, NREL]), ALU.is_equal))
                        v.engine_nop().then_inc(s_rel, 1)
                        link(v.tensor_tensor(vv, vv, falling[:, :].rearrange("p (a r) -> p a r", a=1).to_broadcast([CH, P, NREL]), ALU.mult))
                        link(v.tensor_reduce(top[:, :], vv, AX, ALU.max))
                        link(v.tensor_scalar(relc[:, t * P:(t + 1) * P], top[:, :], -1.0, float(NREL), ALU.mult, ALU.add))

                    for r in range(NREL):
                        for k, m in enumerate((lastm, firstm)):
                            link(v.scalar_tensor_tensor(fwd, relc[:, :], float(r), m[:, :], ALU.is_equal, ALU.mult,
                                                        accum_out=ends[:, k * NREL + r:k * NREL + r + 1]))
                    v.engine_nop().then_inc(s_ev, 1)
                    dve.wait_ge(s_tp, 2)
                    link(v.tensor_copy(endt[:, :, :], ps[0][0:NREL, 0:4, 0:CH]))
                    link(v.memset(carry[:, :, :], 0.0))
                    link(v.tensor_tensor_scan(carry[:, 0, 1:CH + 1], endt[:, 2, :], endt[:, 0, :], 0.0, ALU.mult, ALU.add))
                    link(v.tensor_tensor_scan(carry[:, 1, 0:CH][:, ::-1], endt[:, 3, :][:, ::-1], endt[:, 1, :][:, ::-1], 0.0, ALU.mult, ALU.add))
                    v.engine_nop().then_inc(s_ev, 1)
                    dve.wait_ge(s_tp, 3)
                    link(v.tensor_copy(carc[:, :, :], ps[0][0:CH, 4:6, 0:NREL]))

                    for r in range(NREL):
                        link(v.tensor_scalar(lastm[:, :], relc[:, :], float(r), None, ALU.is_equal))
                        link(v.tensor_tensor_scan(fwd, same[:, 0:CE], lastm[:, :], carc[:, 0, r:r + 1], ALU.mult, ALU.add))
                        link(v.tensor_tensor_scan(bwd[:, ::-1], same[:, 1:CE + 1][:, ::-1], lastm[:, ::-1], carc[:, 1, r:r + 1], ALU.mult, ALU.add))
                        link(v.tensor_tensor(fwd, fwd, bwd, ALU.add))
                        if r == 0:
                            link(v.tensor_tensor(tot, fwd, lastm[:, :], ALU.mult))
                        else:
                            link(v.tensor_tensor(fwd, fwd, lastm[:, :], ALU.mult))
                            link(v.tensor_tensor(tot, tot, fwd, ALU.add))
                    link(v.tensor_scalar(tot, tot, -1.0, 1.0, ALU.add, ALU.max))
                    link(v.reciprocal(tot, tot))
                    dve.wait_ge(s_src, 16)
                    link(v.tensor_copy(fwd, raw[:, :]))
                    link(v.scalar_tensor_tensor(bwd, fwd, float(NREL), relc[:, :], ALU.mult, ALU.add))
                    link(v.memset(src_i[:, TILES:], 0))
                    v.engine_nop().then_inc(s_ev, 1)
                    n = 0
                    for to in (dst_f, wgt, src_i, rel_i):
                        view = to[:, 0:TILES].rearrange("e (p t) -> e t p", t=CT)
                        for b in range(CT // 5):
                            dve.wait_ge(s_tp, 4 + n)
                            v.tensor_copy(view[:, 5 * b:5 * b + 5, :], ps[n % 2][:, 0:5, 0:CH]).then_inc(s_pe, 1)
                            n += 1

                @block.tensor
                def _(pe):
                    t = nc.tensor
                    pe.wait_ge(s_ev, 1)
                    t.matmul(psf[:, 0:512], ones[0:1, :], fin[0:1, 0:512], start=True, stop=True)
                    t.matmul(psf[:, 512:GROUPS], ones[0:1, :], fin[0:1, 512:GROUPS], start=True, stop=True).then_inc(s_tp, 1)
                    pe.wait_ge(s_ev, 2)
                    for k in range(4):
                        last = t.transpose(ps[0][0:NREL, k, 0:CH], ends[:, k * NREL:(k + 1) * NREL], ident[0:CH, 0:CH])
                    last.then_inc(s_tp, 1)
                    pe.wait_ge(s_ev, 3)
                    t.transpose(ps[0][0:CH, 4, 0:NREL], carry[:, 0, 0:CH], ident[0:NREL, 0:NREL])
                    t.transpose(ps[0][0:CH, 5, 0:NREL], carry[:, 1, 1:CH + 1], ident[0:NREL, 0:NREL]).then_inc(s_tp, 1)
                    pe.wait_ge(s_ev, 4)
                    n = 0
                    for of in (dstc, tot, fwd, bwd):
                        for b in range(CT // 5):
                            if n >= 2:
                                pe.wait_ge(s_pe, n - 1)
                            for q in range(5):
                                c0 = (5 * b + q) * P
                                last = t.transpose(ps[n % 2][:, q, 0:CH], of[:, c0:c0 + P], ident[0:CH, 0:CH])
                            last.then_inc(s_tp, 1)
                            n += 1

        def tables(name, first, norm, wcols, load_w, bias_in, save_x1):
            nt = wcols - D
            dest = ytab if nt > D else xltab
            with ExitStack() as st:
                wt = sbuf(st, f"{name}_w", [P, wcols])
                brow = sbuf(st, f"{name}_b", [P, D]) if bias_in is not None else None
                xt = [sbuf(st, f"{name}_x{k}", [P, D]) for k in range(2)]
                stat = [sbuf(st, f"{name}_st{k}", [P, nc.vector.BN_STATS_DIM]) for k in range(2)]
                mv = [sbuf(st, f"{name}_mv{k}", [P, 4]) for k in range(2)]
                hn = [sbuf(st, f"{name}_hn{k}", [P, D]) for k in range(2)]
                ht = [sbuf(st, f"{name}_ht{k}", [P, P]) for k in range(2)]
                eps = sbuf(st, f"{name}_eps", [P, 1])
                yb = [sbuf(st, f"{name}_y{k}", [P, nt]) for k in range(2)]
                pt = [psum(st, f"{name}_pt{k}", [P, 512]) for k in range(2)]
                py = [psum(st, f"{name}_py{k}", [P, 1536]) for k in range(2)]
                s_w, s_eps = sem(f"{name}_w_in"), sem(f"{name}_eps_set")
                s_x = [sem(f"{name}_x_in{k}") for k in range(2)]
                s_st, s_var = sem(f"{name}_stats"), sem(f"{name}_variance")
                s_std, s_rs = sem(f"{name}_std"), sem(f"{name}_rstd")
                s_hn, s_t = sem(f"{name}_rows"), sem(f"{name}_turned")
                s_ht, s_mm = sem(f"{name}_relu"), sem(f"{name}_product")
                s_ya, s_yd = sem(f"{name}_copied_act"), sem(f"{name}_copied_dve")
                s_add = sem(f"{name}_added")
                s_out = [sem(f"{name}_stored{k}") for k in range(2)]
                s_x1 = sem(f"{name}_x1_stored")
                uses_x = first or bias_in is not None
                full = wcols // 512 * 512
                if full > nt:
                    full = 0

                def a_tile(i):
                    return A[:, ds(i * D, D)]

                with nc.Block() as block:

                    @block.sync
                    def _(sp):
                        n_w = load_w(sp, wt, brow, s_w)

                        def load(j, k, rows=P):
                            i = 2 * j + k
                            sp.dma_start(xt[k][0:rows, :], x[ds(i * P, rows), :]).then_inc(s_x[k], 16)

                        def use(j, k):
                            return (s_hn if first else s_yd, 2 * j + k - 1)

                        if uses_x:
                            load(0, 0)
                            load(0, 1)
                            with sp.Fori(1, NT // 2 - 1) as j:
                                for k in range(2):
                                    gate(sp, "sp", use(j, k))
                                    load(j, k)
                            j = NT // 2 - 1
                            for k in range(2):
                                gate(sp, "sp", use(j, k))
                                load(j, k, P if k == 0 else LAST)
                        elif save_x1:
                            def save(j, k):
                                i = 2 * j + k
                                sp.dma_start(x1_dram[ds(i * P, P), :], a_tile(i)).then_inc(s_x[k], 16)
                            save(0, 0)
                            save(0, 1)
                            with sp.Fori(1, NT // 2) as j:
                                for k in range(2):
                                    gate(sp, "sp", (s_x[k], 16 * j))
                                    save(j, k)

                    @block.gpsimd
                    def _(pool):
                        def store(j, k):
                            i = 2 * j + k
                            gate(pool, "pool", (s_yd, i + 1), (s_ya, i + 1))
                            pool.dma_start(dest[ds(i * P, P), :], yb[k][:, :]).then_inc(s_out[k], 16)
                        with pool.Fori(0, NT // 2) as j:
                            for k in range(2):
                                store(j, k)
                        for k in range(2):
                            pool.wait_ge(s_out[k], 16 * (NT // 2))
                        if save_x1:
                            for k in range(2):
                                pool.wait_ge(s_x[k], 16 * (NT // 2))

                    @block.vector
                    def _(dve):
                        v = nc.vector
                        v.memset(eps[:, :], EPS).then_inc(s_eps, 1)

                        def relu_rows(j, k, i, peel):
                            if not peel:
                                gate(dve, "dve", (s_t, i - 1))
                            v.tensor_scalar(hn[k][:, :], a_tile(i), 0.0, None, ALU.max).then_inc(s_hn, 1)

                        def normalise(j, k, i, peel):
                            if first:
                                gate(dve, "dve", (s_x[k], 16 * (j + 1)))
                                rows = xt[k][:, :]
                            else:
                                rows = a_tile(i)
                            v.bn_stats(stat[k][:, :], rows).then_inc(s_st, 1)
                            gate(dve, "dve", (s_st, i + 1))
                            v.bn_aggr(mv[k][:, 0:2], stat[k][:, :]).then_inc(s_var, 1)

                        def normalise_end(j, k, i, peel):
                            rows = xt[k][:, :] if first else a_tile(i)
                            gate(dve, "dve", (s_std, i + 1))
                            v.reciprocal(mv[k][:, 3:4], mv[k][:, 2:3]).then_inc(s_rs, 1)
                            if peel:
                                gate(dve, "dve", (s_rs, i + 1))
                            else:
                                gate(dve, "dve", (s_rs, i + 1), (s_t, i - 1))
                            v.tensor_scalar(hn[k][:, :], rows, mv[k][:, 0:1], mv[k][:, 3:4],
                                            ALU.subtract, ALU.mult).then_inc(s_hn, 1)

                        def finish(j, k, i, peel):
                            gate(dve, "dve", (s_mm, i + 1))
                            if not peel:
                                gate(dve, "dve", (s_out[k], 16 * j))
                            v.tensor_copy(yb[k][:, full:nt], py[k][:, full:nt])
                            if save_x1:
                                gate(dve, "dve", (s_x[k], 16 * (j + 1)))
                                v.tensor_copy(a_tile(i), py[k][:, nt:wcols]).then_inc(s_yd, 1)
                            elif first:
                                v.tensor_tensor(a_tile(i), py[k][:, nt:wcols], brow[:, :], ALU.add).then_inc(s_yd, 1)
                            else:
                                gate(dve, "dve", (s_x[k], 16 * (j + 1)))
                                v.tensor_tensor(a_tile(i), py[k][:, nt:wcols], brow[:, :], ALU.add).then_inc(s_add, 1)
                                gate(dve, "dve", (s_add, i + 1))
                                v.tensor_tensor(a_tile(i), a_tile(i), xt[k][:, :], ALU.add).then_inc(s_yd, 1)

                        def pair(j, peel):
                            if norm:
                                for k in range(2):
                                    normalise(j, k, 2 * j + k, peel)
                                for k in range(2):
                                    normalise_end(j, k, 2 * j + k, peel)
                            else:
                                for k in range(2):
                                    relu_rows(j, k, 2 * j + k, peel)
                            for k in range(2):
                                finish(j, k, 2 * j + k, peel)
                        if brow is not None:
                            dve.wait_ge(s_w, 16 * 3)
                        pair(0, True)
                        with dve.Fori(1, NT // 2) as j:
                            pair(j, False)

                    @block.scalar
                    def _(act):
                        a = nc.scalar
                        act.wait_ge(s_eps, 1)

                        def pair(j, peel):
                            if norm:
                                for k in range(2):
                                    gate(act, "act", (s_var, 2 * j + k + 1))
                                    a.activation(mv[k][:, 2:3], mv[k][:, 1:2], ACT.Sqrt, bias=eps[:, 0:1]).then_inc(s_std, 1)
                            for k in range(2):
                                i = 2 * j + k
                                gate(act, "act", (s_t, i + 1))
                                if not peel:
                                    gate(act, "act", (s_mm, i - 1))
                                a.activation(ht[k][:, :], pt[k][:, 0:P], ACT.Relu).then_inc(s_ht, 1)
                            for k in range(2):
                                i = 2 * j + k
                                gate(act, "act", (s_mm, i + 1))
                                if full:
                                    if not peel:
                                        gate(act, "act", (s_out[k], 16 * j))
                                    a.activation(yb[k][:, 0:full], py[k][:, 0:full], ACT.Copy).then_inc(s_ya, 1)
                                else:
                                    act.sem_inc(s_ya)
                        pair(0, True)
                        with act.Fori(1, NT // 2) as j:
                            pair(j, False)

                    @block.tensor
                    def _(pe):
                        t = nc.tensor
                        pe.wait_ge(s_w, 16 * (3 if brow is not None else 2))

                        def pair(j, peel):
                            for k in range(2):
                                i = 2 * j + k
                                gate(pe, "pe", (s_hn, i + 1))
                                if not peel:
                                    gate(pe, "pe", (s_ht, i - 1))
                                t.transpose(pt[k][:, 0:P], hn[k][:, :], ident[:, :]).then_inc(s_t, 1)
                            for k in range(2):
                                i = 2 * j + k
                                gate(pe, "pe", (s_ht, i + 1))
                                if not peel:
                                    gate(pe, "pe", (s_yd, i - 1), (s_ya, i - 1))
                                for c in range(0, wcols, 512):
                                    e = min(c + 512, wcols)
                                    last = t.matmul(py[k][:, c:e], ht[k][:, :], wt[:, c:e], start=True, stop=True)
                                last.then_inc(s_mm, 1)
                        pair(0, True)
                        with pe.Fori(1, NT // 2) as j:
                            pair(j, False)

        def rgcn_weights(w_rel, root, b):
            def load(sp, wt, brow, s):
                sp.dma_start(wt[:, 0:NREL * D].rearrange("d (r o) -> d r o", r=NREL),
                             w_rel.rearrange("r d o -> d r o")).then_inc(s, 16)
                sp.dma_start(wt[:, NREL * D:ALL], root).then_inc(s, 16)
                sp.dma_start(brow[:, :], b.rearrange("(a d) -> a d", a=1).to_broadcast([P, D])).then_inc(s, 16)
            return load

        def gat_weights(sp, wt, brow, s):
            sp.dma_start(wt[:, 0:D], w_l).then_inc(s, 16)
            sp.dma_start(wt[:, D:2 * D], w_r).then_inc(s, 16)

        def sum_engines(block, name, onehot, dloc, pg, V, width, s_v, s_pe):
            s_dl, s_oh, s_acc = sem(f"{name}_local"), sem(f"{name}_onehot"), sem(f"{name}_summed")

            @block.vector
            def _(dve):
                v = nc.vector

                def pair(i, peel):
                    for k in range(2):
                        s = 2 * i + k
                        dcol = dve.value_load(steps[0:1, ds(4 * s + 2, 1)], min_val=0, max_val=TILES - G)
                        v.tensor_scalar(dloc[k][:, :], dst_f[:, ds(dcol, G)], base[:, ds(s, 1)], None,
                                        ALU.subtract).then_inc(s_dl, 1)
                        gate(dve, "dve", (s_dl, s + 1))
                        if not peel:
                            gate(dve, "dve", (s_pe, s - 1))
                        v.tensor_tensor(onehot[k][:, :].rearrange("p (t n) -> p t n", t=G),
                                        cols[:, :].rearrange("p (a n) -> p a n", a=1).to_broadcast([P, G, P]),
                                        dloc[k][:, :].rearrange("p (t a) -> p t a", a=1).to_broadcast([P, G, P]),
                                        ALU.is_equal).then_inc(s_oh, 1)
                    for k in range(2):
                        s = 2 * i + k
                        n = dve.value_load(steps[0:1, ds(4 * s + 3, 1)], min_val=0, max_val=NT - 1)
                        gate(dve, "dve", (s_pe, s + 1))
                        if not (peel and k == 0):
                            gate(dve, "dve", (s_acc, s))
                        to = A[:, ds(n * width, width)]
                        v.tensor_tensor(to, pg[k][:, 0:width], to, ALU.add).then_inc(s_acc, 1)
                pair(0, True)
                with dve.Fori(1, STEPS // 2) as i:
                    pair(i, False)

            @block.tensor
            def _(pe):
                t = nc.tensor

                def pair(i, peel):
                    for k in range(2):
                        s = 2 * i + k
                        gp1 = pe.value_load(steps[0:1, ds(4 * s, 1)], min_val=1, max_val=GROUPS)
                        slot = pe.value_load(steps[0:1, ds(4 * s + 1, 1)], min_val=0, max_val=SLOTS - 1)
                        gate(pe, "pe", (s_oh, s + 1))
                        gate(pe, "pe", (s_v, gp1))
                        if not peel:
                            gate(pe, "pe", (s_acc, s - 1))
                        for q in range(G):
                            last = t.matmul(pg[k][:, 0:width], onehot[k][:, q * P:(q + 1) * P],
                                            V[:, ds(slot * (G * width) + q * width, width)],
                                            start=(q == 0), stop=(q == G - 1))
                        last.then_inc(s_pe, 1)
                pair(0, True)
                with pe.Fori(1, STEPS // 2) as i:
                    pair(i, False)

        def gather_engine(block, rows, stage, gbuf, s_stage, s_g, s_free, s_kept=None):
            @block.gpsimd
            def _(pool):
                def round_(i, peel):
                    for k in range(SLOTS):
                        if peel:
                            pool.wait_ge(s_stage, k + 1)
                        else:
                            gate(pool, "pool", (s_free, SLOTS * (i - 1) + k + 1))
                            if s_kept is not None:
                                gate(pool, "pool", (s_kept[k], 16 * i))
                        for q in range(G):
                            pool.indirect_dma_start(
                                gbuf[k][:, q * D:(q + 1) * D], None, rows,
                                bass.IndirectOffsetOnAxis(ap=stage[k][:, q:q + 1], axis=0)).then_inc(s_g[k], 16)
                round_(0, True)
                with pool.Fori(1, ROUNDS) as i:
                    round_(i, False)

        def rgcn_pass(name):
            with ExitStack() as st:
                gbuf = [sbuf(st, f"{name}_g{k}", [P, G * D]) for k in range(SLOTS)]
                stage = [sbuf(st, f"{name}_i{k}", [P, G], I32) for k in range(SLOTS)]
                V = sbuf(st, f"{name}_v", [P, SLOTS * G * D])
                onehot = [sbuf(st, f"{name}_oh{k}", [P, G * P]) for k in range(2)]
                dloc = [sbuf(st, f"{name}_dl{k}", [P, G]) for k in range(2)]
                pg = [psum(st, f"{name}_pg{k}", [P, 512]) for k in range(2)]
                s_stage, s_v, s_pe = sem(f"{name}_staged"), sem(f"{name}_scaled"), sem(f"{name}_multiplied")
                s_g = [sem(f"{name}_gathered{k}") for k in range(SLOTS)]
                with nc.Block() as block:
                    gather_engine(block, ytab.rearrange("n (r d) -> (n r) d", d=D), stage, gbuf, s_stage, s_g, s_v)
                    sum_engines(block, name, onehot, dloc, pg, V, D, s_v, s_pe)

                    @block.scalar
                    def _(act):
                        a = nc.scalar
                        for k in range(SLOTS):
                            a.activation(stage[k][:, :], rel_i[:, k * G:(k + 1) * G], ACT.Copy).then_inc(s_stage, 1)

                        def round_(i, peel):
                            for k in range(SLOTS):
                                g = SLOTS * i + k
                                gate(act, "act", (s_g[k], 16 * G * (i + 1)))
                                a.activation(stage[k][:, :], rel_i[:, ds(G * g + G * SLOTS, G)], ACT.Copy)
                                if not peel:
                                    upto = act.value_load(done[0:1, ds(g - SLOTS, 1)], min_val=1, max_val=STEPS)
                                    gate(act, "act", (s_pe, upto))
                                for q in range(G):
                                    c = (k * G + q) * D
                                    last = a.activation(V[:, c:c + D], gbuf[k][:, q * D:(q + 1) * D], ACT.Copy,
                                                        scale=wgt[:, ds(G * g + q, 1)])
                                last.then_inc(s_v, 1)
                        round_(0, True)
                        with act.Fori(1, ROUNDS) as i:
                            round_(i, False)

        def score_pass(sc):
            with ExitStack() as st:
                gbuf = [sbuf(st, f"a_g{k}", [P, GD]) for k in range(SLOTS)]
                stage = [sbuf(st, f"a_i{k}", [P, G], I32) for k in range(SLOTS)]
                Z = sbuf(st, "a_z", [P, SLOTS * GD])
                dall = sbuf(st, "a_dst", [P, SLOTS * GE], I32)
                onehot = [sbuf(st, f"a_oh{k}", [P, GE]) for k in range(2)]
                L = sbuf(st, "a_leaky", [P, GD])
                attb = sbuf(st, "attb", [P, D])
                node = sbuf(st, "node", [P, SCOLS * P])
                pg = [psum(st, f"a_pg{k}", [P, 8 * P]) for k in range(2)]
                s_att, s_stage, s_z = sem("a_att_in"), sem("a_staged"), sem("a_copied")
                s_g = [sem(f"a_gathered{k}") for k in range(SLOTS)]
                s_d = [sem(f"a_dst_in{k}") for k in range(SLOTS)]
                s_kept = [sem(f"a_stored{k}") for k in range(SLOTS)]
                s_oh, s_pe, s_add = sem("a_onehot"), sem("a_multiplied"), sem("a_added")
                s_lk, s_wt, s_done = sem("a_leaky_done"), sem("a_weighted"), sem("a_scored")
                with nc.Block() as block:
                    gather_engine(block, xltab, stage, gbuf, s_stage, s_g, s_z, s_kept)

                    @block.sync
                    def _(sp):
                        sp.dma_start(attb[:, :], att.rearrange("(a h) c -> a (h c)", a=1).to_broadcast([P, D])).then_inc(s_att, 16)

                        def round_(i, peel):
                            for k in range(SLOTS):
                                g = SLOTS * i + k
                                if not peel:
                                    upto = sp.value_load(done[0:1, ds(g - SLOTS, 1)], min_val=1, max_val=STEPS)
                                    gate(sp, "sp", (s_done, upto))
                                sp.dma_start(dall[:, k * GE:(k + 1) * GE],
                                             dst.rearrange("(a e) -> a e", a=1)[:, ds(g * GE, GE)].to_broadcast([P, GE])).then_inc(s_d[k], 16)
                                gate(sp, "sp", (s_g[k], 16 * G * (i + 1)))
                                sp.dma_start(xj_dram[ds(g, 1), :, :].rearrange("a p c -> p (a c)"), gbuf[k][:, :]).then_inc(s_kept[k], 16)
                        round_(0, True)
                        with sp.Fori(1, ROUNDS) as i:
                            round_(i, False)
                        for k in range(SLOTS):
                            sp.wait_ge(s_kept[k], 16 * ROUNDS)

                    @block.scalar
                    def _(act):
                        a = nc.scalar
                        for k in range(SLOTS):
                            a.activation(stage[k][:, :], src_i[:, k * G:(k + 1) * G], ACT.Copy).then_inc(s_stage, 1)

                        def round_(i, peel):
                            for k in range(SLOTS):
                                g = SLOTS * i + k
                                gate(act, "act", (s_g[k], 16 * G * (i + 1)))
                                a.activation(stage[k][:, :], src_i[:, ds(G * g + G * SLOTS, G)], ACT.Copy)
                                gate(act, "act", (s_d[k], 16 * (i + 1)))
                                if not peel:
                                    upto = act.value_load(done[0:1, ds(g - SLOTS, 1)], min_val=1, max_val=STEPS)
                                    gate(act, "act", (s_done, upto))
                                a.activation(Z[:, k * GD:(k + 1) * GD], gbuf[k][:, :], ACT.Copy).then_inc(s_z, 1)
                        round_(0, True)
                        with act.Fori(1, ROUNDS) as i:
                            round_(i, False)

                    @block.vector
                    def _(dve):
                        v = nc.vector
                        dve.wait_ge(s_att, 16)
                        v.tensor_scalar(node[:, :], base[:, :], rowid[:, 0:1], None, ALU.add).then_inc(s_add, 1)
                        dve.wait_ge(s_add, 1)

                        def pair(i, peel):
                            for k in range(2):
                                s = 2 * i + k
                                gp1 = dve.value_load(steps[0:1, ds(4 * s, 1)], min_val=1, max_val=GROUPS)
                                slot = dve.value_load(steps[0:1, ds(4 * s + 1, 1)], min_val=0, max_val=SLOTS - 1)
                                gate(dve, "dve", (s_z, gp1))
                                if not peel:
                                    gate(dve, "dve", (s_pe, s - 1))
                                v.tensor_scalar(onehot[k][:, :], dall[:, ds(slot * GE, GE)], node[:, ds(s, 1)], None,
                                                ALU.is_equal).then_inc(s_oh, 1)
                            for k in range(2):
                                s = 2 * i + k
                                slot = dve.value_load(steps[0:1, ds(4 * s + 1, 1)], min_val=0, max_val=SLOTS - 1)
                                dcol = dve.value_load(steps[0:1, ds(4 * s + 2, 1)], min_val=0, max_val=TILES - G)
                                z = Z[:, ds(slot * GD, GD)]
                                gate(dve, "dve", (s_pe, s + 1))
                                v.tensor_tensor(z, pg[k][:, 0:GD], z, ALU.add).then_inc(s_add, 1)
                                gate(dve, "dve", (s_add, s + 2))
                                v.scalar_tensor_tensor(L[:, :], z, SLOPE, z, ALU.mult, ALU.max).then_inc(s_lk, 1)
                                gate(dve, "dve", (s_lk, s + 1))
                                v.tensor_tensor(L[:, :].rearrange("p (t d) -> p t d", t=G), L[:, :].rearrange("p (t d) -> p t d", t=G),
                                                attb[:, :].rearrange("p (a d) -> p a d", a=1).to_broadcast([P, G, D]),
                                                ALU.mult).then_inc(s_wt, 1)
                                gate(dve, "dve", (s_wt, s + 1))
                                v.tensor_reduce(sc[:, ds(dcol * H, G * H)], L[:, :].rearrange("p (t c) -> p t c", c=C),
                                                AX, ALU.add).then_inc(s_done, 1)
                        pair(0, True)
                        with dve.Fori(1, STEPS // 2) as i:
                            pair(i, False)

                    @block.tensor
                    def _(pe):
                        t = nc.tensor

                        def pair(i, peel):
                            for k in range(2):
                                s = 2 * i + k
                                n = pe.value_load(steps[0:1, ds(4 * s + 3, 1)], min_val=0, max_val=NT - 1)
                                gate(pe, "pe", (s_oh, s + 1))
                                if not peel:
                                    gate(pe, "pe", (s_add, s))
                                for q in range(G):
                                    last = t.matmul(pg[k][:, q * D:(q + 1) * D], onehot[k][:, q * P:(q + 1) * P],
                                                    A[:, ds(n * D, D)], start=True, stop=True)
                                last.then_inc(s_pe, 1)
                        pair(0, True)
                        with pe.Fori(1, STEPS // 2) as i:
                            pair(i, False)

        def softmax_weights(sc):
            with ExitStack() as st:
                raw = src_i[0:CH, :]
                score = [A[0:CH, h * CE:(h + 1) * CE] for h in range(H)]
                fwd = sbuf(st, "m_fwd", [CH, CE])
                bwd = sbuf(st, "m_bwd", [CH, CE])
                apart = sbuf(st, "m_apart", [CH, CE + 1], BF16)
                notlast = sbuf(st, "m_notlast", [CH, CE], BF16)
                notfirst = sbuf(st, "m_notfirst", [CH, CE], BF16)
                edge_i = sbuf(st, "m_edge_i", [CH, 2], I32)
                edge_f = sbuf(st, "m_edge_f", [CH, 2])
                ends = sbuf(st, "m_ends", [CH, 4 * H])
                endt = sbuf(st, "m_endt", [H, 4, CH])
                carry = sbuf(st, "m_carry", [H, 2, CH + 1])
                carc = sbuf(st, "m_carc", [CH, 2, H])
                ps = [psum(st, f"m_ps{k}", [P, 8, P]) for k in range(2)]
                s_dst, s_nb, s_const = sem("m_dst_in"), sem("m_neighbours"), sem("m_const")
                s_tp, s_ev, s_free, s_top, s_exp = sem("m_turned"), sem("m_to_turn"), sem("m_psum_free"), sem("m_relative"), sem("m_exp")
                scv = sc[:, :].rearrange("e (p t h) -> e t h p", t=CT, h=H)
                NB = CT // 5
                with nc.Block() as block:

                    @block.sync
                    def _(sp):
                        sp.dma_start(raw, dst.rearrange("(p e) -> p e", p=CH)).then_inc(s_dst, 16)
                        sp.wait_ge(s_const, 1)
                        with nc.allow_non_contiguous_dma(reason="one destination of each chunk"):
                            sp.dma_start(edge_i[1:CH, 0:1], dst.rearrange("(p e) -> p e", p=CH)[0:CH - 1, CE - 1:CE]).then_inc(s_nb, 16)
                            sp.dma_start(edge_i[0:CH - 1, 1:2], dst.rearrange("(p e) -> p e", p=CH)[1:CH, 0:1]).then_inc(s_nb, 16)

                    @block.scalar
                    def _(act):
                        for h in range(H):
                            act.wait_ge(s_top, h + 1)
                            nc.scalar.activation(score[h], score[h], ACT.Exp).then_inc(s_exp, 1)

                    @block.vector
                    def _(dve):
                        link = Chain(dve, "m_chain")
                        v = nc.vector
                        v.memset(edge_i[:, :], -1).then_inc(s_const, 1)
                        dve.wait_ge(s_dst, 16)
                        link(v.tensor_copy(fwd[:, :], raw))
                        dve.wait_ge(s_nb, 32)
                        link(v.tensor_copy(edge_f[:, :], edge_i[:, :]))
                        link(v.tensor_tensor(apart[:, 1:CE], fwd[:, 1:CE], fwd[:, 0:CE - 1], ALU.not_equal))
                        link(v.tensor_scalar(apart[:, 0:1], fwd[:, 0:1], edge_f[:, 0:1], None, ALU.not_equal))
                        link(v.tensor_scalar(apart[:, CE:CE + 1], fwd[:, CE - 1:CE], edge_f[:, 1:2], None, ALU.not_equal))
                        link(v.tensor_scalar(apart[:, :], apart[:, :], -BIG, None, ALU.mult))
                        link(v.tensor_scalar(notfirst[:, :], fwd[:, :], fwd[:, 0:1], -BIG, ALU.not_equal, ALU.mult))
                        link(v.tensor_scalar(notlast[:, :], fwd[:, :], fwd[:, CE - 1:CE], -BIG, ALU.not_equal, ALU.mult))
                        for k, (c, c0) in enumerate(((CE - 1, CE - H), (0, 0))):
                            e = ends[:, (2 + k) * H:(3 + k) * H]
                            link(v.tensor_scalar(e, fwd[:, c0:c0 + H], 0.0, fwd[:, c:c + 1], ALU.mult, ALU.add))
                            link(v.tensor_scalar(e, e, edge_f[:, k:k + 1], -BIG, ALU.not_equal, ALU.mult))
                        n = 0
                        for h in range(H):
                            for b in range(NB):
                                dve.wait_ge(s_tp, n + 1)
                                v.tensor_copy(score[h][:, 5 * b * P:(5 * b + 5) * P].rearrange("p (q e) -> p q e", q=5),
                                              ps[n % 2][0:CH, 0:5, :]).then_inc(s_free, 1)
                                n += 1
                        dve.wait_ge(s_free, n)
                        for h in range(H):
                            for k, m in enumerate((notlast, notfirst)):
                                link(v.tensor_tensor_reduce(bwd[:, :], score[h], m[:, :], 1.0, -BIG, ALU.add, ALU.max,
                                                            ends[:, k * H + h:k * H + h + 1]))
                        v.engine_nop().then_inc(s_ev, 1)
                        dve.wait_ge(s_tp, n + 1)
                        link(v.tensor_copy(endt[:, :, :], ps[0][0:H, 0:4, 0:CH]))
                        link(v.memset(carry[:, :, :], -BIG))
                        link(v.tensor_tensor_scan(carry[:, 0, 1:CH + 1], endt[:, 2, :], endt[:, 0, :], -BIG, ALU.add, ALU.max))
                        link(v.tensor_tensor_scan(carry[:, 1, 0:CH][:, ::-1], endt[:, 3, :][:, ::-1], endt[:, 1, :][:, ::-1], -BIG, ALU.add, ALU.max))
                        v.engine_nop().then_inc(s_ev, 1)
                        dve.wait_ge(s_tp, n + 2)
                        link(v.tensor_copy(carc[:, :, :], ps[0][0:CH, 4:6, 0:H]))
                        for h in range(H):
                            link(v.tensor_tensor_scan(fwd[:, :], apart[:, 0:CE], score[h], carc[:, 0, h:h + 1], ALU.add, ALU.max))
                            link(v.tensor_tensor_scan(bwd[:, ::-1], apart[:, 1:CE + 1][:, ::-1], score[h][:, ::-1], carc[:, 1, h:h + 1], ALU.add, ALU.max))
                            link(v.tensor_tensor(fwd[:, :], fwd[:, :], bwd[:, :], ALU.max))
                            link(v.tensor_tensor(score[h], score[h], fwd[:, :], ALU.subtract))
                            v.engine_nop().then_inc(s_top, 1)
                        m = n
                        for h in range(H):
                            for b in range(NB):
                                dve.wait_ge(s_tp, m + 3)
                                v.tensor_copy(scv[:, 5 * b:5 * b + 5, h, :], ps[m % 2][:, 0:5, 0:CH]).then_inc(s_free, 1)
                                m += 1

                    @block.tensor
                    def _(pe):
                        t = nc.tensor
                        n = 0
                        for h in range(H):
                            for b in range(NB):
                                if n >= 2:
                                    pe.wait_ge(s_free, n - 1)
                                for q in range(5):
                                    last = t.transpose(ps[n % 2][0:CH, q, :], scv[:, 5 * b + q, h, :], ident[:, :])
                                last.then_inc(s_tp, 1)
                                n += 1
                        pe.wait_ge(s_free, n)
                        pe.wait_ge(s_ev, 1)
                        for k in range(4):
                            last = t.transpose(ps[0][0:H, k, 0:CH], ends[:, k * H:(k + 1) * H], ident[0:CH, 0:CH])
                        last.then_inc(s_tp, 1)
                        pe.wait_ge(s_ev, 2)
                        t.transpose(ps[0][0:CH, 4, 0:H], carry[:, 0, 0:CH], ident[0:H, 0:H])
                        t.transpose(ps[0][0:CH, 5, 0:H], carry[:, 1, 1:CH + 1], ident[0:H, 0:H]).then_inc(s_tp, 1)
                        for h in range(H):
                            pe.wait_ge(s_exp, h + 1)
                            for b in range(NB):
                                pe.wait_ge(s_free, n - 1 if h or b >= 2 else H * NB)
                                for q in range(5):
                                    c0 = (5 * b + q) * P
                                    last = t.transpose(ps[n % 2][:, q, 0:CH], score[h][:, c0:c0 + P], ident[0:CH, 0:CH])
                                last.then_inc(s_tp, 1)
                                n += 1

        def attend(sc):
            with ExitStack() as st:
                rows = [sbuf(st, f"s_x{k}", [P, GD]) for k in range(SLOTS)]
                V = sbuf(st, "s_v", [P, SLOTS * G * W])
                onehot = [sbuf(st, f"s_oh{k}", [P, G * P]) for k in range(2)]
                dloc = [sbuf(st, f"s_dl{k}", [P, G]) for k in range(2)]
                pg = [psum(st, f"s_pg{k}", [P, 512]) for k in range(2)]
                s_x = [sem(f"s_rows_in{k}") for k in range(SLOTS)]
                s_v, s_pe = sem("s_scaled"), sem("s_multiplied")
                with nc.Block() as block:
                    @block.vector
                    def _(dve):
                        nc.vector.memset(A[:, :], 0.0)
                with nc.Block() as block:
                    sum_engines(block, "s", onehot, dloc, pg, V, W, s_v, s_pe)

                    @block.sync
                    def _(sp):
                        def round_(i, peel):
                            for k in range(SLOTS):
                                g = SLOTS * i + k
                                if not peel:
                                    gate(sp, "sp", (s_v, g - SLOTS + 1))
                                sp.dma_start(rows[k][:, :], xj_dram[ds(g, 1), :, :].rearrange("a p c -> p (a c)")).then_inc(s_x[k], 16)
                        round_(0, True)
                        with sp.Fori(1, ROUNDS) as i:
                            round_(i, False)

                    @block.gpsimd
                    def _(pool):
                        q = nc.gpsimd

                        def round_(i, peel):
                            for k in range(SLOTS):
                                g = SLOTS * i + k
                                gate(pool, "pool", (s_x[k], 16 * (i + 1)))
                                if not peel:
                                    upto = pool.value_load(done[0:1, ds(g - SLOTS, 1)], min_val=1, max_val=STEPS)
                                    gate(pool, "pool", (s_pe, upto))
                                to = V[:, k * G * W:(k + 1) * G * W].rearrange("p (t w) -> p t w", t=G)
                                e = sc[:, ds(G * H * g, G * H)].rearrange("p (t h) -> p t h", t=G)
                                q.tensor_tensor(to[:, :, 0:D].rearrange("p t (h c) -> p t h c", h=H),
                                                rows[k][:, :].rearrange("p (t h c) -> p t h c", t=G, h=H),
                                                e.rearrange("p t (h a) -> p t h a", a=1).to_broadcast([P, G, H, C]), ALU.mult)
                                q.tensor_copy(to[:, :, D:W], e).then_inc(s_v, 1)
                        round_(0, True)
                        with pool.Fori(1, ROUNDS) as i:
                            round_(i, False)

        def finish():
            B = 7
            with ExitStack() as st:
                den = sbuf(st, "o_den", [P, NT, H])
                biasb = sbuf(st, "o_bias", [P, D])
                xin = [sbuf(st, f"o_x{k}", [P, B * D]) for k in range(2)]
                res = [sbuf(st, f"o_r{k}", [P, B * D]) for k in range(2)]
                s_b = sem("o_bias_in")
                s_x = [sem(f"o_x_in{k}") for k in range(2)]
                s_o = [sem(f"o_stored{k}") for k in range(2)]
                s_r, s_use = sem("o_ready"), sem("o_x_used")
                Av = A[:, :].rearrange("p (i w) -> p i w", w=W)
                xv = x1_dram.rearrange("(i p) d -> p i d", p=P)
                with nc.Block() as block:

                    @block.sync
                    def _(sp):
                        sp.dma_start(biasb[:, :], bias.rearrange("(a d) -> a d", a=1).to_broadcast([P, D])).then_inc(s_b, 16)
                        for b in range(NT // B):
                            if b >= 2:
                                sp.wait_ge(s_use, b - 1)
                            sp.dma_start(xin[b % 2][:, :].rearrange("p (i d) -> p i d", d=D), xv[:, b * B:(b + 1) * B, :]).then_inc(s_x[b % 2], 16)

                    @block.scalar
                    def _(act):
                        count = [0, 0]
                        for b in range(NT // B):
                            k, full = b % 2, B if b < NT // B - 1 else B - 1
                            act.wait_ge(s_r, b + 1)
                            r0 = b * B * P
                            act.dma_start(out[r0:r0 + full * P, :].rearrange("(i p) d -> p i d", p=P),
                                          res[k][:, 0:full * D].rearrange("p (i d) -> p i d", d=D)).then_inc(s_o[k], 16)
                            count[k] += 16
                            if full < B:
                                act.dma_start(out[(NT - 1) * P:N, :], res[k][0:LAST, full * D:]).then_inc(s_o[k], 16)
                                count[k] += 16
                        for k in range(2):
                            act.wait_ge(s_o[k], count[k])

                    @block.vector
                    def _(dve):
                        link = Chain(dve, "o_chain")
                        v = nc.vector
                        link(v.tensor_scalar(den[:, :, :], Av[:, :, D:W], 1e-16, None, ALU.add))
                        link(v.reciprocal(den[:, :, :], den[:, :, :]))
                        dve.wait_ge(s_b, 16)
                        for b in range(NT // B):
                            k = b % 2
                            dve.wait_ge(s_x[k], 16 * (b // 2 + 1))
                            if b >= 2:
                                dve.wait_ge(s_o[k], 16 * (b // 2))
                            r = res[k][:, :]
                            link(v.tensor_tensor(r.rearrange("p (i h c) -> p i h c", i=B, h=H),
                                                 Av[:, b * B:(b + 1) * B, 0:D].rearrange("p i (h c) -> p i h c", h=H),
                                                 den[:, b * B:(b + 1) * B, :].rearrange("p i (h a) -> p i h a", a=1).to_broadcast([P, B, H, C]),
                                                 ALU.mult))
                            link(v.tensor_tensor(r, r, xin[k][:, :], ALU.add))
                            v.engine_nop().then_inc(s_use, 1)
                            v.tensor_tensor(r.rearrange("p (i d) -> p i d", d=D), r.rearrange("p (i d) -> p i d", d=D),
                                            biasb[:, :].rearrange("p (a d) -> p a d", a=1).to_broadcast([P, B, D]), ALU.add).then_inc(s_r, 1)

        if stop >= 1:
            tables("t1", True, True, ALL, rgcn_weights(w_rel1, root1, b1), b1, False)
        if stop >= 2:
            rgcn_pass("p1")
        if stop >= 3:
            tables("t2", False, False, ALL, rgcn_weights(w_rel2, root2, b2), b2, False)
        if stop >= 4:
            rgcn_pass("p2")
        if stop < 5:
            return dump(nc, outer, sem, A, out)
        relational.close()
        tables("t3", False, True, 2 * D, gat_weights, None, True)
        sc = sbuf(outer, "scores", [P, TILES * H])
        score_pass(sc)
        softmax_weights(sc)
        attend(sc)
        finish()


def ring_steps():
    step = SLOTS
    while step * 2 < GROUPS:
        step *= 2
    while step >= SLOTS:
        yield step
        step //= 2


def dump(nc, outer, sem, A, out):
    s = sem("dumped")
    with nc.Block() as block:
        @block.sync
        def _(sp):
            sp.dma_start(out[0:(NT - 1) * P, :].rearrange("(i p) d -> p i d", p=P),
                         A[:, 0:(NT - 1) * D].rearrange("p (i d) -> p i d", d=D)).then_inc(s, 16)
            sp.dma_start(out[(NT - 1) * P:N, :], A[0:LAST, (NT - 1) * D:NT * D]).then_inc(s, 16)
            sp.wait_ge(s, 32)


STOP = 99
_INS = ["x", "src", "dst", "edge_attr_42", "L0_gnn_w_rel1", "L0_gnn_root1", "L0_gnn_b1", "L0_gnn_w_rel2",
        "L0_gnn_root2", "L0_gnn_b2", "L1_gnn_W_l", "L1_gnn_W_r", "L1_gnn_att", "L1_gnn_bias"]


def kernel(**inputs):
    import numpy as _np
    import concourse.bacc as _bacc
    from concourse.bass_utils import run_bass_kernel_spmd as _run

    nc = _bacc.Bacc("TRN2", target_bir_lowering=False, num_devices=1)
    arrays, args = {}, []
    for name in _INS:
        a = _np.ascontiguousarray(inputs[name])
        arrays[f"in_{name}_dram"] = a
        args.append(nc.dram_tensor(f"in_{name}_dram", a.shape, mybir.dt.from_np(a.dtype), kind="ExternalInput").ap())
    args.append(nc.dram_tensor("out_0_dram", (N, D), F32, kind="ExternalOutput").ap())
    scratch = [("ytab", (NT * P, NREL * D), F32), ("xltab", (NT * P, D), F32), ("x1_dram", (NT * P, D), F32),
               ("xj_dram", (GROUPS, P, G * D), F32), ("step_dram", (SCOLS * P, 4), I32), ("base_dram", (SCOLS * P,), F32)]
    for name, shape, dt in scratch:
        args.append(nc.dram_tensor(name, shape, dt, kind="Internal").ap())
    build(nc, *args, stop=STOP)
    r = _run(nc, [arrays], core_ids=[0])
    return r.results[0]["out_0_dram"]
```
